# Optimizing a Trainium2 kernel written in Bass

```python
import numpy as np
import jax
import jax.numpy as jnp

def _softmax(x, axis=-1):
    return jax.nn.softmax(x, axis=axis)

def _gelu(x):
    return jax.nn.gelu(x, approximate=True)

def _silu(x):
    return jax.nn.silu(x)

def _sigmoid(x):
    return jax.nn.sigmoid(x)

def _layernorm(x, axis=-1, eps=1e-05):
    m = jnp.mean(x, axis=axis, keepdims=True)
    v = jnp.var(x, axis=axis, keepdims=True)
    return (x - m) / jnp.sqrt(v + eps)

def _scatter_add(tgt, idx, src, axis=0):
    return tgt.at[idx].add(src)

def _segment_sum(src, seg, n):
    return jax.ops.segment_sum(src, seg, n)
kernel_name = 'mk_recurrent_d1_jaxref_r4_a2ee0a'

def setup_inputs(seed: int=0):
    np.random.seed(seed)
    _w = jnp.asarray

    def _L0_attn_setup():
        import math
        import jax, jax.numpy as jnp
        import numpy as np
        B, T, E = (2, 512, 1024)
        H, HKV = (32, 8)
        DH = E // H
        G = H // HKV
        ROPE_THETA = 500000.0
        ROPE_FACTOR = 32.0
        HI_FREQ_FACTOR = 4.0
        LO_FREQ_FACTOR = 1.0
        ORIG_CTX = 2048

        def _rope_cos_sin(t_len):
            inv_freq = 1.0 / ROPE_THETA ** (jnp.arange(0, DH, 2, dtype=jnp.float32) / DH)
            wavelen = 2.0 * math.pi / inv_freq
            cut_lo = ORIG_CTX / HI_FREQ_FACTOR
            cut_hi = ORIG_CTX / LO_FREQ_FACTOR
            inv_freq = jnp.where(wavelen > cut_hi, inv_freq / ROPE_FACTOR, inv_freq)
            smooth = (ORIG_CTX / wavelen - LO_FREQ_FACTOR) / (HI_FREQ_FACTOR - LO_FREQ_FACTOR)
            smoothed = (1.0 - smooth) * inv_freq / ROPE_FACTOR + smooth * inv_freq
            is_medium = ~(wavelen < cut_hi) & ~(wavelen > cut_lo)
            inv_freq = jnp.where(is_medium, smoothed, inv_freq)
            pos = jnp.arange(t_len, dtype=jnp.float32)
            freqs = pos[:, None] * inv_freq[None, :]
            emb = jnp.concatenate([freqs, freqs], axis=-1)
            return (jnp.cos(emb), jnp.sin(emb))

        def _rotate_half(x):
            x1, x2 = jnp.split(x, 2, axis=-1)
            return jnp.concatenate([-x2, x1], axis=-1)
        key = jax.random.key(seed)
        kx, kq, kk, kv, ko = jax.random.split(key, 5)
        w = lambda k, shape: jax.random.normal(k, shape, jnp.float32) * 0.02
        return {'x': jax.random.normal(kx, (B, T, E), jnp.float32), 'Wq': w(kq, (E, E)), 'Wk': w(kk, (HKV * DH, E)), 'Wv': w(kv, (HKV * DH, E)), 'Wo': w(ko, (E, E))}
    _L0_attn_in = _L0_attn_setup()

    def _L0_ffn_setup():
        import jax, jax.numpy as jnp
        import numpy as np
        B, S, K, N = (4, 512, 1024, 1024)
        key = jax.random.key(seed)
        k1, k2, k3, k4 = jax.random.split(key, 4)
        x = jax.random.normal(k1, (B, S, K), dtype=jnp.float32)
        qw = jax.random.randint(k2, (N, K), -128, 128, dtype=jnp.int32)
        sw = jax.random.uniform(k3, (), dtype=jnp.float32) * 0.02 + 0.001
        bias = jax.random.normal(k4, (N,), dtype=jnp.float32)
        return {'x': x, 'qw': qw, 'sw': sw, 'bias': bias}
    _L0_ffn_in = _L0_ffn_setup()
    _d = {'L0_attn_x': _L0_attn_in['x'], 'L0_attn_Wq': _L0_attn_in['Wq'], 'L0_attn_Wk': _L0_attn_in['Wk'], 'L0_attn_Wv': _L0_attn_in['Wv'], 'L0_attn_Wo': _L0_attn_in['Wo'], 'L0_ffn_qw': _L0_ffn_in['qw'], 'L0_ffn_sw': _L0_ffn_in['sw'], 'L0_ffn_bias': _L0_ffn_in['bias']}
    _x0 = _d['L0_attn_x']
    _d['L0_attn_x'] = jax.random.normal(jax.random.fold_in(jax.random.key(seed), 1), (2, 2048, 1024), dtype=_x0.dtype)
    del _x0
    return _d

def reference(L0_attn_x, L0_attn_Wq, L0_attn_Wk, L0_attn_Wv, L0_attn_Wo, L0_ffn_qw, L0_ffn_sw, L0_ffn_bias):

    def _L0_attn_ref(x, Wq, Wk, Wv, Wo):
        import math
        import jax, jax.numpy as jnp
        import numpy as np
        B, T, E = (2, 512, 1024)
        H, HKV = (32, 8)
        DH = E // H
        G = H // HKV
        ROPE_THETA = 500000.0
        ROPE_FACTOR = 32.0
        HI_FREQ_FACTOR = 4.0
        LO_FREQ_FACTOR = 1.0
        ORIG_CTX = 2048

        def _rope_cos_sin(t_len):
            inv_freq = 1.0 / ROPE_THETA ** (jnp.arange(0, DH, 2, dtype=jnp.float32) / DH)
            wavelen = 2.0 * math.pi / inv_freq
            cut_lo = ORIG_CTX / HI_FREQ_FACTOR
            cut_hi = ORIG_CTX / LO_FREQ_FACTOR
            inv_freq = jnp.where(wavelen > cut_hi, inv_freq / ROPE_FACTOR, inv_freq)
            smooth = (ORIG_CTX / wavelen - LO_FREQ_FACTOR) / (HI_FREQ_FACTOR - LO_FREQ_FACTOR)
            smoothed = (1.0 - smooth) * inv_freq / ROPE_FACTOR + smooth * inv_freq
            is_medium = ~(wavelen < cut_hi) & ~(wavelen > cut_lo)
            inv_freq = jnp.where(is_medium, smoothed, inv_freq)
            pos = jnp.arange(t_len, dtype=jnp.float32)
            freqs = pos[:, None] * inv_freq[None, :]
            emb = jnp.concatenate([freqs, freqs], axis=-1)
            return (jnp.cos(emb), jnp.sin(emb))

        def _rotate_half(x):
            x1, x2 = jnp.split(x, 2, axis=-1)
            return jnp.concatenate([-x2, x1], axis=-1)
        b, t, _ = x.shape
        q = (x @ Wq.T).reshape(b, t, H, DH).transpose(0, 2, 1, 3)
        k = (x @ Wk.T).reshape(b, t, HKV, DH).transpose(0, 2, 1, 3)
        v = (x @ Wv.T).reshape(b, t, HKV, DH).transpose(0, 2, 1, 3)
        cos, sin = _rope_cos_sin(t)
        cos = cos.astype(x.dtype)[None, None]
        sin = sin.astype(x.dtype)[None, None]
        q = q * cos + _rotate_half(q) * sin
        k = k * cos + _rotate_half(k) * sin
        qg = q.reshape(b, HKV, G, t, DH)
        scores = jnp.einsum('bhgtd,bhkd->bhgtk', qg.astype(jnp.float32), k.astype(jnp.float32)) / math.sqrt(DH)
        causal = jnp.tril(jnp.ones((t, t), dtype=bool))
        scores = jnp.where(causal[None, None, None], scores, jnp.finfo(jnp.float32).min)
        attn = jax.nn.softmax(scores, axis=-1).astype(x.dtype)
        ctx = jnp.einsum('bhgtk,bhkd->bhgtd', attn, v)
        out = ctx.reshape(b, H, t, DH).transpose(0, 2, 1, 3).reshape(b, t, E)
        return out @ Wo.T

    def _L0_ffn_ref(x, qw, sw, bias):
        import jax, jax.numpy as jnp
        import numpy as np
        B, S, K, N = (4, 512, 1024, 1024)
        x_dtype = x.dtype
        w = qw.astype(jnp.float32) * sw
        y = jnp.einsum('bsk,nk->bsn', x.astype(jnp.float32), w).astype(x_dtype)
        y = y + bias
        return y
    x = L0_attn_x
    xn = _layernorm(x, axis=-1)
    s = _L0_attn_ref(xn, L0_attn_Wq, L0_attn_Wk, L0_attn_Wv, L0_attn_Wo)
    g = _silu(_L0_ffn_ref(xn, L0_ffn_qw, L0_ffn_sw, L0_ffn_bias))
    x = x + s * g
    return x

_drawn_inputs = setup_inputs


def setup_inputs(seed=0):
    import zlib

    import numpy as np

    out = dict(_drawn_inputs(seed))
    spreads = {}
    factors = {'L0_ffn_bias': 3.946}
    for name, (base, spread) in spreads.items():
        noise = np.random.default_rng([zlib.crc32(name.encode()), seed]).standard_normal(out[name].shape)
        drawn = base * np.exp(spread * noise) if base else spread * noise
        out[name] = jnp.asarray(drawn.astype(out[name].dtype))
    for name, factor in factors.items():
        out[name] = (out[name] * factor).astype(out[name].dtype)
    return out
```

```python
from contextlib import ExitStack

import numpy as np

import concourse.bass as bass
from concourse import mybir

F32 = mybir.dt.float32
F16 = mybir.dt.float16
BF16 = mybir.dt.bfloat16
I32 = mybir.dt.int32
ALU = mybir.AluOpType
ACT = mybir.ActivationFunctionType
AX = mybir.AxisListType

P = 128
B, T, E = 2, 2048, 1024
H, HKV, DH = 32, 8, 32
G = H // HKV
KC = E // P
TB = 512
NTOK = B * T
NBLK = NTOK // TB
NQB = T // TB
TT = TB // P
NQKV = E + 2 * HKV * DH
QT = E // P
KT = HKV * DH // P
QK = QT + KT
EPS = 1e-5
NEWTON = 4

X_UP = 2.0 ** 10
Q_DOWN = 2.0 ** -23
V_DOWN = 2.0 ** -21
M_UNIT = 2.0 ** 15
FP16_WHOLE = 2 ** 11
W_EXP = 14
MASK = -3.0e38


def rope_tables():
    f = np.float32
    inv = f(1.0) / np.power(f(500000.0), np.arange(0, DH, 2, dtype=f) / f(DH)).astype(f)
    wavelen = f(2.0 * np.pi) / inv
    lo, hi = f(2048 / 4.0), f(2048 / 1.0)
    freq = np.where(wavelen > hi, inv / f(32.0), inv).astype(f)
    smooth = (f(2048) / wavelen - f(1.0)) / f(3.0)
    smoothed = (f(1.0) - smooth) * freq / f(32.0) + smooth * freq
    medium = ~(wavelen < hi) & ~(wavelen > lo)
    freq = np.where(medium, smoothed, freq).astype(f)
    angle = (np.arange(T, dtype=f)[None, :] * freq[:, None]).astype(f)
    cos, sin = np.cos(angle), np.sin(angle)
    cos = np.concatenate([cos, cos], 0)
    sin = np.concatenate([-sin, sin], 0)
    both = np.stack([np.tile(cos, (G, 1)), np.tile(sin, (G, 1))], 1).astype(f)
    return np.tile(both.reshape(P, 2, NQB, TB).transpose(2, 0, 1, 3), (B, 1, 1, 1))


class Ring:

    def __init__(self, slots, n):
        self.slots, self.n = slots, n

    def slot(self, k):
        return k % self.n % self.slots

    def back(self, k):
        k %= self.n
        d = 1
        while (k - d) % self.n % self.slots != k % self.slots:
            d += 1
        return d


def build_constants(nc, c):
    ready = c["sem"]("constants_ready")
    with nc.Block() as block:

        @block.gpsimd
        def _(pool):
            n = 0
            for t in (c["ident16"], c["identb"], c["mask_qk"]):
                pool.memset(t[:, :], 0.0).then_inc(ready, 1)
                n += 1
            pool.wait_ge(ready, n)
            for t in (c["ident16"], c["identb"]):
                pool.affine_select(out=t[:, :], in_=t[:, :], compare_op=ALU.not_equal, fill=1.0, base=0,
                                   pattern=[[-1, P]], channel_multiplier=1).then_inc(ready, 1)
                n += 1
            pool.affine_select(out=c["mask_qk"][:, :], in_=c["mask_qk"][:, :], compare_op=ALU.is_ge, fill=MASK,
                               base=0, pattern=[[-1, P]], channel_multiplier=1).then_inc(ready, 1)
            pool.wait_ge(ready, n + 1)


def prepare_weights(nc, c, matrices, unit, inv, wo_pairs):
    tiles = [(m, r) for m, (w, _, _, _) in enumerate(matrices) for r in range(w.shape[0] // P)]
    first = {}
    for n, (m, r) in enumerate(tiles):
        first.setdefault(m, n)
    NM, NT = len(matrices), len(tiles)
    rows = [w.shape[0] // P for w, _, _, _ in matrices]
    whole = NM - 1
    with ExitStack() as stack:
        sb = lambda name, shape, dt: stack.enter_context(nc.sbuf_tensor(name, shape, dt))
        sem = lambda name: stack.enter_context(nc.semaphore(name))
        raw = sb("raw", [P, max(s + r for (_, _, _, s), r in zip(matrices, rows)), E], F32)
        high = sb("high", [P, 2, E], F16)
        rest = sb("rest", [P, 2, E], F16)
        amax = sb("amax", [P, NT], F32)
        mmax = sb("mmax", [P, NM], F32)
        gmax = sb("gmax", [P, NM], F32)
        expo = sb("expo", [P, NM], I32)
        inf = sb("inf", [P, NM], F32)
        turned = [stack.enter_context(nc.psum_tensor(f"turned{i}", [P, KC, P], F16)) for i in range(4)]
        loaded = [sem(f"loaded{m}") for m in range(NM)]
        chain, mmax_ready, gmax_ready, unit_ready = sem("chain"), sem("mmax_ready"), sem("gmax_ready"), sem("unit_ready")
        high_ready, rest_ready, turned_ready, floats = sem("high_ready"), sem("rest_ready"), sem("turned_ready"), sem("floats")
        high_out = sem("high_out")
        rest_out = [sem(f"rest_out{i}") for i in range(2)]
        wo_stored = sem("wo_stored")
        block = stack.enter_context(nc.Block())

        def raw_tile(n):
            m, r = tiles[n]
            return raw[:, matrices[m][3] + r, :]

        def out_tile(n, part):
            m, r = tiles[n]
            col = matrices[m][2] + r * P
            return matrices[m][1][:, part, :, col:col + P]

        @block.sync
        def _(sp):
            for m, (w, _, _, slot) in enumerate(matrices):
                dst = raw[:, slot:slot + rows[m], :]
                if m == whole:
                    dst = dst.bitcast(I32)
                    sp.wait_ge(rest_ready, rows[0])
                    sp.wait_ge(high_ready, rows[0])
                sp.dma_start(dst, w.rearrange("(r p) k -> p r k", p=P)).then_inc(loaded[m], 16)
            wo = [m for m in range(NM) if matrices[m][1] is c["w_out"]][0]
            end = first[wo] + rows[wo]
            sp.wait_ge(high_out, end)
            for parity in range(2):
                sp.wait_ge(rest_out[parity], (end + 1 - parity) // 2)
            sp.dma_start(wo_pairs, c["w_out"][:, :, :, :]).then_inc(wo_stored, 16)
            sp.wait_ge(wo_stored, 16)

        @block.gpsimd
        def _(pool):
            for m in range(NM):
                if m == whole:
                    pool.wait_ge(loaded[m], 16)
                    for r in range(rows[m]):
                        t = raw_tile(first[m] + r)
                        nc.gpsimd.tensor_copy(t, t.bitcast(I32)).then_inc(floats, 1)
                pool.wait_ge(mmax_ready, m + 1)
                pool.partition_all_reduce(gmax[:, m:m + 1], mmax[:, m:m + 1], P,
                                          bass.bass_isa.ReduceOp.absmax).then_inc(gmax_ready, 1)

        @block.vector
        def _(dve):
            done = [0]

            def link(ins):
                done[0] += 1
                ins.then_inc(chain, 1)
                dve.wait_ge(chain, done[0])

            def maxima(m):
                if m < whole:
                    dve.wait_ge(loaded[m], 16)
                for r in range(rows[m]):
                    n = first[m] + r
                    if m == whole:
                        dve.wait_ge(floats, r + 1)
                    ins = nc.vector.tensor_reduce(out=amax[:, n:n + 1], in_=raw_tile(n), axis=AX.X, op=ALU.max,
                                                  apply_absolute_value=True)
                link(ins)
                nc.vector.reduce_max(mmax[:, m:m + 1], amax[:, first[m]:first[m] + rows[m]],
                                     AX.X).then_inc(mmax_ready, 1)

            def scale(m):
                dve.wait_ge(gmax_ready, m + 1)
                g, e = gmax[:, m:m + 1], expo[:, m:m + 1]
                if m == whole:
                    nc.vector.tensor_scalar(c["gate_rest"][:, :], g, float(FP16_WHOLE), None, ALU.is_gt)
                link(nc.vector.tensor_scalar(g, g, 2.0 ** -60, None, ALU.max))
                link(nc.vector.tensor_tensor(e, g.bitcast(I32), inf[:, m:m + 1].bitcast(I32), ALU.bitwise_and))
                nc.vector.tensor_scalar(inv[:, m:m + 1].bitcast(I32), e, float(W_EXP << 23), None, ALU.subtract)
                nc.vector.tensor_scalar(unit[:, m:m + 1].bitcast(I32), e, -1.0, float((254 + W_EXP) << 23),
                                        ALU.mult, ALU.add).then_inc(unit_ready, 1)
                dve.wait_ge(unit_ready, m + 1)

            def evacuate(n):
                if n % 2 == 0:
                    dve.wait_ge(turned_ready, n + 1)
                    nc.vector.tensor_copy(out_tile(n, 1), turned[1][:, :, :]).then_inc(rest_out[0], 1)

            link(nc.vector.memset(inf[:, :], float("inf")))
            maxima(0)
            for m in range(NM):
                if m == whole:
                    maxima(m)
                elif m + 1 != whole:
                    maxima(m + 1)
                scale(m)
                for r in range(rows[m]):
                    n = first[m] + r
                    dve.wait_ge(high_ready, n + 1)
                    if n >= 2:
                        dve.wait_ge(turned_ready, n - 1)
                    nc.vector.scalar_tensor_tensor(out=rest[:, n % 2, :], in0=raw_tile(n), scalar=unit[:, m:m + 1],
                                                   in1=high[:, n % 2, :], op0=ALU.mult,
                                                   op1=ALU.subtract).then_inc(rest_ready, 1)
                    if n >= 1:
                        evacuate(n - 1)
            evacuate(NT - 1)

        @block.scalar
        def _(act):
            for n in range(NT + 1):
                if n < NT:
                    m, r = tiles[n]
                    if r == 0:
                        act.wait_ge(unit_ready, m + 1)
                    if n >= 2:
                        act.wait_ge(turned_ready, n - 1)
                        act.wait_ge(rest_ready, n - 1)
                    nc.scalar.activation(high[:, n % 2, :], raw_tile(n), ACT.Copy,
                                         scale=unit[:, m:m + 1]).then_inc(high_ready, 1)
                if n >= 1:
                    act.wait_ge(turned_ready, n)
                    nc.scalar.activation(out_tile(n - 1, 0), turned[2 * ((n - 1) % 2)][:, :, :],
                                         ACT.Copy).then_inc(high_out, 1)
                    if (n - 1) % 2:
                        nc.scalar.activation(out_tile(n - 1, 1), turned[3][:, :, :], ACT.Copy).then_inc(rest_out[1], 1)

        @block.tensor
        def _(pe):
            for n in range(NT):
                pe.wait_ge(high_ready, n + 1)
                pe.wait_ge(rest_ready, n + 1)
                if n >= 2:
                    pe.wait_ge(high_out, n - 1)
                    pe.wait_ge(rest_out[n % 2], n // 2)
                for half, src in enumerate((high, rest)):
                    for k in range(KC):
                        last = nc.tensor.transpose(turned[2 * (n % 2) + half][:, k, :], src[:, n % 2, k * P:(k + 1) * P],
                                                   c["ident16"][:, :])
                last.then_inc(turned_ready, 1)



A_GROUPS = [("qk", k) for k in range(QK)] + [("v", t) for t in range(TT)] + [("gate", k) for k in range(2 * TT)]
GAP = len(A_GROUPS) // TT
AROUND = {GAP * t + lag: (kind, t) for t in range(TT) for kind, lag in (("ln", 0), ("split", 1), ("turn", 4))}
A_STEPS = [s for g, step in enumerate(A_GROUPS) for s in ((AROUND[g], step) if g in AROUND else (step,))]
A_FIRST = [(kind, t) for t in range(TT) for kind in ("ln", "split", "turn")]
GROUPS = QK + TT + 2 * TT
ACC = 4
QS, VS, ZS = 4, 2, 4


def phase_a(nc, c, x, tables, q_dram, k_dram, v_dram, g_dram):
    wt, wf = c["w_qkv"], c["w_gate"]
    with ExitStack() as stack:
        sb = lambda name, shape, dt: stack.enter_context(nc.sbuf_tensor(name, shape, dt))
        sem = lambda name: stack.enter_context(nc.semaphore(name))
        xin = sb("xin", [P, TT, E], F32)
        xn = sb("xn", [P, E], F32)
        xhigh = sb("xhigh", [P, E], F16)
        xrest = sb("xrest", [P, E], F16)
        xt = sb("xt", [P, 2, 2, KC, TB], F16)
        stats = sb("stats", [P, 2, 6], F32)
        mv = sb("mv", [P, 2], F32)
        rstd = sb("rstd", [P, 1], F32)
        newton = sb("newton", [P, 1], F32)
        cs = sb("cs", [P, 2, 2, TB], F32)
        qraw = sb("qraw", [P, 2, TB], F32)
        rot = sb("rot", [P, TB], F32)
        qcos = sb("qcos", [P, TB], F32)
        pair = sb("pair", [P, QS, 2, TB], F16)
        vout = sb("vout", [P, VS, HKV * DH], F32)
        z = sb("z", [P, ZS, TB], F32)
        gout = sb("gout", [P, ZS, TB], F32)
        acc = [stack.enter_context(nc.psum_tensor(f"acc{i}", [P, TB], F32)) for i in range(ACC)]
        tp = [stack.enter_context(nc.psum_tensor(f"tp{i}", [P, KC, P], F16)) for i in range(2)]
        x_in = [sem(f"x_in{t}") for t in range(TT)]
        cs_in = [sem(f"cs_in{u}") for u in range(2)]
        a_chain = sem("a_chain")
        ln_done, high_done, rest_done, turn_done = sem("ln_done"), sem("high_done"), sem("rest_done"), sem("turn_done")
        high_out, rest_out = sem("high_out"), sem("rest_out")
        group_done, acc_out = sem("group_done"), sem("acc_out")
        pair_done = sem("pair_done")
        bias_done, gate_done = sem("bias_done"), sem("gate_done")
        pair_stored = [sem(f"pair_stored{s}") for s in range(QS)]
        v_stored = [sem(f"v_stored{s}") for s in range(VS)]
        g_stored = [sem(f"g_stored{s}") for s in range(ZS)]
        block = stack.enter_context(nc.Block())
        group = {s: n for n, s in enumerate([s for s in A_STEPS if s[0] in ("qk", "v", "gate")])}

        def over_blocks(eng, body):
            with eng.Fori(0, NBLK // 2 - 1) as i:
                body(i, 0, False)
                body(i, 1, False)
            body(NBLK // 2 - 1, 0, False)
            body(NBLK // 2 - 1, 1, True)

        def steps(last):
            return [s for s in A_STEPS if not (last and s[0] in ("ln", "split", "turn"))]

        passed = sem("passed_a")

        @block.sync
        def _(sp):
            def load_x(nb, t):
                sp.dma_start(xin[:, t, :], x[bass.ds(nb * TB + t * P, P), :]).then_inc(x_in[t], 16)

            def load_tables(nb, u):
                sp.dma_start(cs[:, u, :, :], tables[nb, :, :, :]).then_inc(cs_in[u], 16)

            for stored in (*pair_stored, *v_stored, *g_stored):
                sp.sem_inc(stored, 16)
            for t in range(TT):
                load_x(0, t)
            load_tables(0, 0)

            def body(i, u, last):
                nb = 2 * i + u
                if not last:
                    for t in range(TT):
                        sp.wait_ge(rest_done, nb * TT + t + 1)
                        sp.sem_inc(passed, 1)
                        load_x(nb + 1, t)
                    sp.wait_ge(pair_done, nb * QK + 1)
                    sp.sem_inc(passed, 1)
                    load_tables(nb + 1, 1 - u)
                for s in steps(last):
                    kind, k = s
                    if kind == "qk":
                        n = u * QK + k
                        slot = n % QS
                        sp.wait_ge(pair_done, nb * QK + k + 2)
                        sp.sem_inc(passed, 1)
                        if k < QT:
                            dst = q_dram[k, :, :, bass.ds(nb * TB, TB)]
                        else:
                            dst = k_dram[k - QT, :, :, bass.ds(nb * TB, TB)]
                        sp.dma_start(dst, pair[:, slot, :, :]).then_inc(pair_stored[slot], 16)
                    if kind == "v":
                        sp.wait_ge(acc_out, nb * GROUPS + group["v", k] + 1 + ACC)
                        sp.sem_inc(passed, 1)
                        sp.dma_start(v_dram[:, :, nb * TT + k, :].rearrange("g p d -> p g d"),
                                     vout[:, k % VS, :].rearrange("p (g d) -> p g d", g=HKV)
                                     ).then_inc(v_stored[k % VS], 16)
                    if kind == "gate":
                        sp.wait_ge(gate_done, nb * 2 * TT + k + 2)
                        sp.sem_inc(passed, 1)
                        sp.dma_start(g_dram[bass.ds(nb * TB + k // 2 * P, P), (k % 2) * TB:(k % 2 + 1) * TB],
                                     gout[:, k % ZS, :]).then_inc(g_stored[k % ZS], 16)

            over_blocks(sp, body)
            for s in range(QS):
                sp.wait_ge(pair_stored[s], 16 * (NBLK * QK // QS + 1))
            for s in range(VS):
                sp.wait_ge(v_stored[s], 16 * (NBLK * TT // VS + 1))
            for s in range(ZS):
                sp.wait_ge(g_stored[s], 16 * (NBLK * 2 * TT // ZS + 1))

        @block.gpsimd
        def _(pool):
            def body(i, u, last):
                nb = 2 * i + u
                for k in range(2 * TT):
                    pool.wait_ge(acc_out, nb * GROUPS + group["gate", k] + 1 + ACC)
                    half = c["bias"][:, (k % 2) * TB:(k % 2 + 1) * TB]
                    nc.gpsimd.tensor_tensor(z[:, k % ZS, :], z[:, k % ZS, :], half, ALU.add).then_inc(bias_done, 1)

            over_blocks(pool, body)

        @block.vector
        def _(dve):
            swap = [(d + DH // 2) % DH for d in range(DH)]

            class Chain:
                base, n = 0, 0

                def link(self, ins):
                    self.n += 1
                    ins.then_inc(a_chain, 1)
                    dve.wait_ge(a_chain, self.base + self.n)

            ch = Chain()
            dve.sem_inc(pair_done, 1)

            def ln_step(nb, t):
                dve.wait_ge(x_in[t], 16 * (nb + 1))
                nc.vector.bn_stats(stats[:, 0, :], xin[:, t, 0:TB])
                ch.link(nc.vector.bn_stats(stats[:, 1, :], xin[:, t, TB:E]))
                nc.vector.memset(newton[:, :], 0.0)
                ch.link(nc.vector.bn_aggr(mv[:, :], stats[:, :, :]))
                ch.link(nc.vector.tensor_scalar(mv[:, 1:2], mv[:, 1:2], EPS, None, ALU.add))
                ch.link(nc.vector.tensor_scalar(rstd[:, :].bitcast(I32), mv[:, 1:2].bitcast(I32), -0.5,
                                                float(0x5F3759DF), ALU.mult, ALU.add))
                for step in range(NEWTON):
                    ch.link(nc.vector.scalar_tensor_tensor(out=newton[:, :], in0=rstd[:, :], scalar=mv[:, 1:2],
                                                           in1=rstd[:, :], op0=ALU.mult, op1=ALU.mult))
                    ch.link(nc.vector.tensor_scalar(newton[:, :], newton[:, :], -0.5, 1.5, ALU.mult, ALU.add))
                    ch.link(nc.vector.scalar_tensor_tensor(out=rstd[:, :], in0=rstd[:, :],
                                                           scalar=X_UP if step == NEWTON - 1 else 1.0,
                                                           in1=newton[:, :], op0=ALU.mult, op1=ALU.mult))
                dve.wait_ge(high_done, nb * TT + t)
                nc.vector.tensor_scalar(xn[:, :], xin[:, t, :], mv[:, 0:1], rstd[:, 0:1], ALU.subtract,
                                        ALU.mult).then_inc(ln_done, 1)

            def split_step(nb, t):
                dve.wait_ge(high_done, nb * TT + t + 1)
                dve.wait_ge(turn_done, nb * TT + t)
                nc.vector.tensor_tensor(xrest[:, :], xn[:, :], xhigh[:, :], ALU.subtract).then_inc(rest_done, 1)

            def turn_step(nb, u, t):
                dve.wait_ge(turn_done, nb * TT + t + 1)
                nc.vector.tensor_copy(xt[:, u, 1, :, t * P:(t + 1) * P], tp[1][:, :, :]).then_inc(rest_out, 1)

            def qk_step(i, u, k):
                nb = 2 * i + u
                if k == 0:
                    dve.wait_ge(cs_in[u], 16 * (i + 1))
                dve.wait_ge(acc_out, nb * GROUPS + group["qk", k] + 1 + ACC)
                src = qraw[:, k % 2, :]
                n = u * QK + k
                slot = n % QS
                nc.vector.tensor_tensor(qcos[:, :], src, cs[:, u, 0, :], ALU.mult)
                ch.link(nc.vector.stream_shuffle(rot[:, :], src, swap))
                ch.link(nc.vector.tensor_tensor(rot[:, :], rot[:, :], cs[:, u, 1, :], ALU.mult))
                ins = nc.vector.tensor_tensor(qraw[:, k % 2, :], qcos[:, :], rot[:, :], ALU.add)
                ch.link(ins)
                dve.wait_ge(pair_stored[slot], 16 * (i * (2 * QK // QS) + n // QS + 1))
                ch.link(nc.vector.tensor_copy(pair[:, slot, 0, :], src))
                nc.vector.tensor_tensor(pair[:, slot, 1, :], src, pair[:, slot, 0, :],
                                        ALU.subtract).then_inc(pair_done, 1)

            LN_LINKS, QK_LINKS = 4 + 3 * NEWTON, 4
            for kind, t in A_FIRST:
                if kind == "ln":
                    ln_step(0, t)
                if kind == "split":
                    split_step(0, t)
                if kind == "turn":
                    turn_step(0, 0, t)
            FIRST_LINKS = ch.n
            BLOCK_LINKS = TT * LN_LINKS + QK * QK_LINKS

            def body(i, u, last):
                nb = 2 * i + u
                ch.base, ch.n = FIRST_LINKS + nb * BLOCK_LINKS, 0
                for kind, k in steps(last):
                    if kind == "ln":
                        ln_step(nb + 1, k)
                    if kind == "split":
                        split_step(nb + 1, k)
                    if kind == "turn":
                        turn_step(nb + 1, 1 - u, k)
                    if kind == "qk":
                        qk_step(i, u, k)
                assert last or ch.n == BLOCK_LINKS

            over_blocks(dve, body)

        @block.scalar
        def _(act):
            act.sem_inc(acc_out, ACC)
            act.sem_inc(gate_done, 1)

            def ln_step(nb, t):
                act.wait_ge(ln_done, nb * TT + t + 1)
                act.wait_ge(turn_done, nb * TT + t)
                act.wait_ge(rest_done, nb * TT + t)
                nc.scalar.activation(xhigh[:, :], xn[:, :], ACT.Copy).then_inc(high_done, 1)

            def turn_step(nb, u, t):
                act.wait_ge(turn_done, nb * TT + t + 1)
                nc.scalar.activation(xt[:, u, 0, :, t * P:(t + 1) * P], tp[0][:, :, :], ACT.Copy).then_inc(high_out, 1)

            for kind, t in A_FIRST:
                if kind == "ln":
                    ln_step(0, t)
                if kind == "turn":
                    turn_step(0, 0, t)

            def body(i, u, last):
                nb = 2 * i + u

                def silu(k):
                    act.wait_ge(bias_done, nb * 2 * TT + k + 1)
                    act.wait_ge(g_stored[k % ZS], 16 * (nb * (2 * TT // ZS) + k // ZS + 1))
                    nc.scalar.activation(gout[:, k % ZS, :], z[:, k % ZS, :], ACT.Silu).then_inc(gate_done, 1)

                for kind, k in steps(last):
                    if kind == "ln":
                        ln_step(nb + 1, k)
                    if kind == "turn":
                        turn_step(nb + 1, 1 - u, k)
                    if kind not in ("qk", "v", "gate"):
                        continue
                    g = group[kind, k]
                    bank = (u * GROUPS + g) % ACC
                    if kind == "gate":
                        act.wait_ge(gate_done, nb * 2 * TT + max(k - ZS + 2, 1))
                    act.wait_ge(group_done, nb * GROUPS + g + 1)
                    if kind == "qk":
                        act.wait_ge(pair_done, nb * QK + max(k, 1))
                        nc.scalar.activation(qraw[:, k % 2, :], acc[bank][:, :], ACT.Copy,
                                             scale=Q_DOWN).then_inc(acc_out, 1)
                    if kind == "v":
                        act.wait_ge(v_stored[k % VS], 16 * (nb * (TT // VS) + k // VS + 1))
                        nc.scalar.activation(vout[:, k % VS, :], acc[bank][:, 0:HKV * DH], ACT.Copy,
                                             scale=V_DOWN).then_inc(acc_out, 1)
                    if kind == "gate":
                        nc.scalar.activation(z[:, k % ZS, :], acc[bank][:, :], ACT.Copy,
                                             scale=c["gate_scale"][:, 0:1]).then_inc(acc_out, 1)
                        if k >= 2:
                            silu(k - 2)
                silu(2 * TT - 2)
                silu(2 * TT - 1)

            over_blocks(act, body)

        @block.tensor
        def _(pe):
            def turn_step(nb, u, t):
                pe.wait_ge(high_done, nb * TT + t + 1)
                pe.wait_ge(rest_done, nb * TT + t + 1)
                pe.wait_ge(high_out, nb * TT + t)
                pe.wait_ge(rest_out, nb * TT + t)
                for half, src in enumerate((xhigh, xrest)):
                    for k in range(KC):
                        last = nc.tensor.transpose(tp[half][:, k, :], src[:, k * P:(k + 1) * P], c["ident16"][:, :])
                last.then_inc(turn_done, 1)

            for kind, t in A_FIRST:
                if kind == "turn":
                    turn_step(0, 0, t)

            def products(out, pairs):
                order = [(a, b, k) for k in range(KC) for a, b in ((0, 0), (0, 1), (1, 0))]
                for n, (a, b, k) in enumerate(order):
                    lhsT, rhs = pairs(a, b, k)
                    last = nc.tensor.matmul(out, lhsT, rhs, start=(n == 0), stop=(n == len(order) - 1))
                last.then_inc(group_done, 1)

            def gate_products(out, u, t, half):
                def product(a, b, j, **ends):
                    return nc.tensor.matmul(out, xt[:, u, a, j, t * P:(t + 1) * P],
                                            wf[:, b, j, half * TB:(half + 1) * TB],
                                            start=ends.get("start", False), stop=ends.get("stop", False))

                for j in range(KC):
                    product(0, 0, j, start=(j == 0))
                with pe.If(weights_have_rest):
                    for j in range(KC):
                        product(0, 1, j)
                for j in range(KC):
                    last = product(1, 0, j, stop=(j == KC - 1))
                last.then_inc(group_done, 1)

            weights_have_rest = pe.value_load(c["gate_rest"][0:1, 0:1], min_val=0, max_val=1)

            def body(i, u, last):
                nb = 2 * i + u
                pe.wait_ge(high_out, (nb + 1) * TT)
                pe.wait_ge(rest_out, (nb + 1) * TT)
                for kind, k in steps(last):
                    if kind == "turn":
                        turn_step(nb + 1, 1 - u, k)
                    if kind not in ("qk", "v", "gate"):
                        continue
                    g = group[kind, k]
                    out = acc[(u * GROUPS + g) % ACC]
                    pe.wait_ge(acc_out, nb * GROUPS + g + 1)
                    if kind == "qk":
                        products(out[:, :], lambda a, b, j: (wt[:, a, j, k * P:(k + 1) * P], xt[:, u, b, j, :]))
                    if kind == "v":
                        products(out[:, 0:HKV * DH],
                                 lambda a, b, j: (xt[:, u, a, j, k * P:(k + 1) * P], wt[:, b, j, QK * P:NQKV]))
                    if kind == "gate":
                        t, half = k // 2, k % 2
                        gate_products(out[:, :], u, t, half)

            over_blocks(pe, body)



S1_BANKS, S2_BANKS = 3, 3
NORM_STAGES = 4
P_GEN = 8
SUMS = 3
BUNDLE = 2
NKT = T // P


def max_tiles(qb):
    return [(h, t, c) for c in range(qb + 1) for h in range(G) for t in range(TT)]


SPOTS = 6
TAIL = 2 * G
VALUES_LAG = 1
SUMS_LAG = 4
LEAD_MAX = 68
ROWS_LAG = 9


def maxima_stream():
    out, due, n = [], [], 0
    for qb in range(NQB):
        for k, m in enumerate(max_tiles(qb)):
            if k == ROWS_LAG:
                out += due
                due = []
            out.append(("max", n < LEAD_MAX, qb, *m))
            n += 1
        out += due + [("shift", n <= LEAD_MAX, qb)]
        due = [("rows", n <= LEAD_MAX, qb, 0), ("rows", n <= LEAD_MAX, qb, 1)]
    out += due
    cut = [x[:2] for x in out].index(("max", False))
    return [(x[0], True, *x[2:]) for x in out[:cut]], [(x[0], False, *x[2:]) for x in out[cut:]]


def pieces(stream, parts):
    total, runs, n = sum(x[0] == "max" for x in stream), [[] for _ in range(parts)], 0
    for x in stream:
        runs[min(n * parts // total, parts - 1)].append(x)
        n += x[0] == "max"
    return runs


def group_schedule():
    steps = [(qb, kt) for qb in range(NQB) for kt in range(TT * (qb + 1))]
    ahead, own = maxima_stream()
    turn = steps.index((NQB - 1, 0)) - 1
    spots = iter(pieces(own, SPOTS * turn) + pieces(ahead, SPOTS * (len(steps) - turn) + TAIL))
    middle, end = [[] for _ in range(len(steps) + 1)], [[] for _ in range(len(steps) + 1)]
    for step, (qb, kt) in enumerate(steps):
        full = TT * qb
        last = step - kt + full + TT - 1
        at = min(step + VALUES_LAG, len(steps))
        place = middle if step == last else end
        close = min(last + VALUES_LAG, len(steps))
        place[at].append(("values", qb, kt))
        if kt >= full:
            place[at].append(("sum", qb, kt, 0))
        elif kt % BUNDLE == BUNDLE - 1 and step + SUMS_LAG <= close:
            middle[step + SUMS_LAG].insert(0, ("sum", qb, kt - BUNDLE + 1, BUNDLE))
        elif kt % BUNDLE == BUNDLE - 1:
            middle[close].insert(0, ("sum", qb, kt - BUNDLE + 1, BUNDLE))
    out, norm = [], []
    for step, (qb, kt) in enumerate(steps):
        for h in range(G):
            out += next(spots)
            out.append(("score", qb, kt, h))
            if h == 1:
                out += middle[step]
                if any(s[0] == "values" for s in middle[step]):
                    norm = [("norm", middle[step][-1][1], stage) for stage in range(NORM_STAGES)]
            if h % 2:
                out += next(spots)
            out += norm[:1]
            norm = norm[1:]
        out += end[step]
    for h in range(G):
        out.append(("next", 0, 0, h))
        out += next(spots)
        if h == 1:
            out += end[len(steps)]
    out += middle[len(steps)]
    for stage in range(NORM_STAGES):
        out.append(("norm", NQB - 1, stage))
        out += next(spots)
    assert next(spots, None) is None
    return out


def phase_b(nc, c, q_dram, k_dram, v_dram, ctx_dram, wo_pairs):
    sched = group_schedule()
    NU = B
    items = {kind: [s for s in sched if s[0] == kind] for kind in ("shift", "score", "values", "sum", "norm")}
    items["norm"] = [s for s in items["norm"] if s[2] == 0]
    items["bank"] = [s for s in sched if s[0] in ("max", "rows")]
    bundles = [s for s in items["sum"] if s[3]]
    items["add"] = [("add", n, s[2] + j) for n, s in enumerate(bundles) for j in range(1, s[3])]
    N = {kind: len(v) for kind, v in items.items()}
    with ExitStack() as stack:
        sb = lambda name, shape, dt: stack.enter_context(nc.sbuf_tensor(name, shape, dt))
        sem = lambda name: stack.enter_context(nc.semaphore(name))
        ps = lambda name, shape, dt: stack.enter_context(nc.psum_tensor(name, shape, dt))
        qs = [sb(f"qs{u}", [P, G, T], F16) for u in range(NU)]
        ks = [sb(f"ks{u}", [P, T], F16) for u in range(NU)]
        vs = [sb(f"vs{u}", [P, NKT, DH], F32) for u in range(NU)]
        prob = sb("prob", [P, P_GEN, G, TB], F32)
        psum = sb("psum", [P, SUMS, G, TB], F32)
        mpart = sb("mpart", [P, G * TT, NQB], F32)
        mfull = sb("mfull", [P, G * TT], F32)
        mpair = sb("mpair", [P, G * TT, DH], F16)
        sums_t = sb("sums_t", [P, TB // DH, DH], F32)
        rsum = sb("rsum", [P, TB // DH], F32)
        rden = sb("rden", [P, TB], F32)
        cval = sb("cval", [P, TB], F32)
        cpair = sb("cpair", [P, 2, 2, TB], F16)
        p_max = [ps(f"p_max{i}", [P, TB], F32) for i in range(S1_BANKS)]
        p_sc = [ps(f"p_sc{i}", [P, TB], F32) for i in range(S2_BANKS)]
        p_val = ps("p_val", [P, TB], F32)
        p_sum = ps("p_sum", [P, TB], F32)
        group_in = [sem(f"group_in{u}") for u in range(NU)]
        init_done, masked, wo_in = sem("init_done"), sem("masked"), sem("wo_in")
        max_scored, max_taken = sem("max_scored"), sem("max_taken")
        shift_ready = sem("shift_ready")
        scored, exp_done = sem("scored"), sem("exp_done")
        values_done, tile_added, sums_done, norm_done = sem("values_done"), sem("tile_added"), sem("sums_done"), sem("norm_done")
        b_chain, ctx_ready, passed = sem("b_chain"), sem("ctx_ready"), sem("passed_b")
        ctx_stored = [sem(f"ctx_stored{s}") for s in range(2)]
        block = stack.enter_context(nc.Block())

        sc_ring = Ring(S2_BANKS, NU * N["score"])
        mx_ring = Ring(S1_BANKS, NU * N["bank"])
        first = maxima_stream()[0]
        LEAD = {"bank": sum(s[0] in ("max", "rows") for s in first), "shift": sum(s[0] == "shift" for s in first)}

        def rows_view(bank):
            return p_max[bank][3 * DH:P, :].bitcast(F16).rearrange("p (j q) -> p j q", q=P)

        def over_groups(eng, kinds, body):
            with eng.Fori(0, HKV - 1) as g:
                for u in range(NU):
                    body(g, u, {kind: eng.snap((g * NU + u) * N[kind]) for kind in kinds}, False)
            for u in range(NU):
                body(HKV - 1, u, {kind: ((HKV - 1) * NU + u) * N[kind] for kind in kinds}, u == NU - 1)

        def schedule(last):
            return [s for s in sched if not (last and (s[0] == "next" or s[0] in ("max", "shift", "rows") and s[1]))]

        class Count:

            def __init__(self, before=None):
                self.bank = self.shift = 0
                self.before = before

            def next_bank(self):
                k = self.bank
                self.bank += 1
                return (k, k) if self.before is None else (self.before["bank"] + (k + LEAD["bank"]), k + LEAD["bank"])

            def banks(self):
                return self.bank if self.before is None else self.before["bank"] + (self.bank + LEAD["bank"])

            def shifts(self):
                return self.shift if self.before is None else self.before["shift"] + (self.shift + LEAD["shift"])

        def rows_at(qb, r):
            mine = [s for s in first + sched if s[0] in ("max", "rows")]
            return [s[0] == "rows" and s[2:] == (qb, r) for s in mine].index(True) + 1

        def step_of(qb, kt):
            return sum(TT * (q + 1) for q in range(qb)) + kt

        def readers(step):
            back = step < 0
            _, qb, kt, _ = items["score"][step % (N["score"] // G) * G]
            v = items["values"].index(("values", qb, kt)) + 1 - back * N["values"]
            if kt >= TT * qb:
                return v, items["sum"].index(("sum", qb, kt, 0)) + 1 - back * N["sum"], None
            n, at = [(i, max(kt, b[2] + 1)) for i, b in enumerate(bundles) if b[1] == qb and b[2] <= kt < b[2] + b[3]][0]
            return v, None, items["add"].index(("add", n, at)) + 1 - back * N["add"]

        V_CREDIT, S_CREDIT, A_CREDIT = P_GEN + 1, N["sum"] + 1, N["add"] * G + 1

        def owner(s, u):
            return 1 - u if s[1] else u

        @block.sync
        def _(sp):
            def load(g, u):
                tok = slice(u * T, (u + 1) * T)
                for part, row in ((0, 0), (0, DH), (1, 2 * DH)):
                    sp.dma_start(qs[u][row:row + DH, :, :],
                                 q_dram[g, :, part, tok].rearrange("(h d) t -> d h t", h=G)).then_inc(group_in[u], 16)
                for part, row in ((0, 0), (1, DH), (0, 2 * DH)):
                    sp.dma_start(ks[u][row:row + DH, :], k_dram[g, :, part, tok]).then_inc(group_in[u], 16)
                sp.dma_start(vs[u][:, :, :], v_dram[g, :, u * NKT:(u + 1) * NKT, :]).then_inc(group_in[u], 16)

            for s in range(2):
                sp.sem_inc(ctx_stored[s], 16)
            for u in range(NU):
                load(0, u)
            sp.dma_start(c["w_out"][:, :, :, :], wo_pairs).then_inc(wo_in, 16)

            def body(g, u, before, last):
                for qb in range(NQB):
                    sp.wait_ge(ctx_ready, before["norm"] * 2 + (2 * qb + 3))
                    sp.sem_inc(passed, 1)
                    sp.dma_start(ctx_dram[g, :, :, u * T + qb * TB:u * T + (qb + 1) * TB],
                                 cpair[:, qb % 2, :, :]).then_inc(ctx_stored[qb % 2], 16)
                if not isinstance(g, int):
                    load(g + 1, u)

            over_groups(sp, ["norm"], body)
            sp.wait_ge(wo_in, 16)
            for s in range(2):
                sp.wait_ge(ctx_stored[s], 16 * (HKV * NU * NQB // 2 + 1))

        @block.gpsimd
        def _(pool):
            nc.gpsimd.memset(mpair[:, :, :], 0.0).then_inc(init_done, 1)

            def mask(before, step):
                _, qb, kt, _ = items["score"][step * G]
                off = P * (kt - TT * qb)
                pool.wait_ge(exp_done, before["score"] + (G * (step + 1) + S2_BANKS))
                pool.sem_inc(passed, 1)
                part = prob[:, step % P_GEN, :, off:off + P]
                nc.gpsimd.affine_select(out=part, in_=part, compare_op=ALU.is_ge, fill=0.0, base=0,
                                        pattern=[[0, G], [1, P]], channel_multiplier=-1).then_inc(masked, 1)

            def add_tile(before, qb, kt):
                n = [i for i, b in enumerate(bundles) if b[1] == qb and b[2] <= kt < b[2] + b[3]][0]
                begins = kt == bundles[n][2] + 1
                k = items["add"].index(("add", n, kt))
                step = step_of(qb, kt)
                for h in range(G):
                    total = psum[:, n % SUMS, h, :]
                    pool.wait_ge(exp_done, before["score"] + (G * step + h + 1 + S2_BANKS))
                    if begins and h == 0:
                        pool.wait_ge(sums_done, before["sum"] + (sum_before(n) + S_CREDIT))
                    if not begins:
                        pool.wait_ge(tile_added, before["add"] * G + (G * (k - 1) + h + 1 + A_CREDIT))
                    nc.gpsimd.tensor_tensor(total, prob[:, (step - 1) % P_GEN, h, :] if begins else total,
                                            prob[:, step % P_GEN, h, :], ALU.add).then_inc(tile_added, 1)

            def split_context(before, qb):
                pool.wait_ge(norm_done, before["norm"] + (qb + 2))
                pool.wait_ge(ctx_stored[qb % 2], before["norm"] * 8 + 16 * (qb // 2 + 1))
                pool.sem_inc(passed, 1)
                nc.gpsimd.tensor_copy(cpair[:, qb % 2, 0, :], cval[:, :]).then_inc(ctx_ready, 1)
                pool.wait_ge(ctx_ready, before["norm"] * 2 + (2 * qb + 2))
                nc.gpsimd.tensor_tensor(cpair[:, qb % 2, 1, :], cval[:, :], cpair[:, qb % 2, 0, :],
                                        ALU.subtract).then_inc(ctx_ready, 1)

            pool.sem_inc(ctx_ready, 1)
            pool.sem_inc(tile_added, A_CREDIT)

            def body(g, u, before, last):
                step = 0
                for qb in range(NQB):
                    for kt in range(TT * (qb + 1)):
                        if kt == 1 and qb > 0:
                            split_context(before, qb - 1)
                        if kt >= TT * qb:
                            mask(before, step)
                        elif kt % BUNDLE:
                            add_tile(before, qb, kt)
                        step += 1
                split_context(before, NQB - 1)

            def sum_before(n):
                if n < SUMS:
                    return items["sum"].index(bundles[n - SUMS]) + 1 - N["sum"]
                return items["sum"].index(bundles[n - SUMS]) + 1

            over_groups(pool, ["score", "sum", "add", "norm"], body)

        @block.scalar
        def _(act):
            act.sem_inc(exp_done, S2_BANKS)

            def body(g, u, before, last):
                for n, (_, qb, kt, h) in enumerate(items["score"]):
                    off = P * max(kt - TT * qb, 0)
                    act.wait_ge(scored, before["score"] + (n + 1))
                    if h == 0:
                        step = n // G
                        v_read, s_read, a_read = readers(step - P_GEN)
                        act.wait_ge(values_done, before["values"] + (v_read + V_CREDIT))
                        if a_read is not None:
                            act.wait_ge(tile_added, before["add"] * G + (G * a_read + A_CREDIT))
                        else:
                            act.wait_ge(sums_done, before["sum"] + (s_read + S_CREDIT))
                    nc.scalar.activation(prob[:, n // G % P_GEN, h, off:TB], p_sc[sc_ring.slot(u * N["score"] + n)][:, off:TB],
                                         ACT.Exp, scale=c["exp_scale"][:, 0:1]).then_inc(exp_done, 1)

            over_groups(act, ["score", "values", "sum", "add"], body)

        @block.vector
        def _(dve):
            chain = {"base": 0, "n": 0}

            def link(ins):
                chain["n"] += 1
                ins.then_inc(b_chain, 1)
                dve.wait_ge(b_chain, chain["base"] + chain["n"])

            dve.sem_inc(max_taken, S1_BANKS)
            dve.sem_inc(norm_done, 1)
            for u in range(NU):
                nc.vector.memset(ks[u][3 * DH:P, :], M_UNIT).then_inc(init_done, 1)
            dve.wait_ge(init_done, NU + 1)

            def run(s, cnt, g, u, last):
                kind = s[0]
                if kind in ("max", "rows"):
                    m, k = cnt.next_bank()
                    bank = mx_ring.slot(k if g is None else u * N["bank"] + k)
                    dve.wait_ge(max_scored, m + 1)
                if kind == "max":
                    _, _, qb, h, t, cb = s
                    width = TB if cb < qb else P * (t + 1)
                    nc.vector.reduce_max(mpart[:, h * TT + t, cb:cb + 1], p_max[bank][:, 0:width],
                                         AX.X).then_inc(max_taken, 1)
                if kind == "shift":
                    qb = s[2]
                    dve.wait_ge(max_taken, cnt.banks() + S1_BANKS)
                    link(nc.vector.reduce_max(mfull[:, :], mpart[:, :, 0:qb + 1], AX.X))
                    link(nc.vector.tensor_scalar(mfull[:, :], mfull[:, :], -1.0 / M_UNIT, None, ALU.mult))
                    link(nc.vector.tensor_copy(mpair[:, :, 0], mfull[:, :]))
                    nc.vector.tensor_tensor(mpair[:, :, 1], mfull[:, :], mpair[:, :, 0],
                                            ALU.subtract).then_inc(shift_ready, 1)
                    cnt.shift += 1
                if kind == "rows":
                    _, _, qb, r = s
                    dst = qs[0 if g is None else owner(s, u)][3 * DH:P, 2 * r:2 * r + 2, qb * TB:(qb + 1) * TB]
                    nc.vector.tensor_copy(dst, rows_view(bank).rearrange("p (h t) q -> p h (t q)", h=2)
                                          ).then_inc(max_taken, 1)
                if kind == "norm" and s[2] == 0:
                    qb = s[1]
                    before = cnt.before
                    dve.wait_ge(values_done, before["values"] + (items["values"].index(("values", qb, TT * (qb + 1) - 1)) + 1 + V_CREDIT))
                    dve.wait_ge(sums_done, before["sum"] + (max(i for i, x in enumerate(items["sum"]) if x[1] == qb) + 1 + S_CREDIT))
                    link(nc.vector.transpose(sums_t[:, :, :].rearrange("p a b -> p (a b)"), p_sum[:, :]))
                    nc.vector.reciprocal(rsum[:, :], sums_t[:, :, 0]).then_inc(b_chain, 1)
                    chain["n"] += 1
                if kind == "norm" and s[2] > 0:
                    dve.wait_ge(b_chain, chain["base"] + chain["n"])
                if kind == "norm" and s[2] == 1:
                    nc.vector.tensor_copy(sums_t[:, :, :],
                                          rsum[:, :].rearrange("p (a b) -> p a b", b=1).broadcast_to([P, TB // DH, DH])
                                          ).then_inc(b_chain, 1)
                    chain["n"] += 1
                if kind == "norm" and s[2] == 2:
                    nc.vector.transpose(rden[:, :], sums_t[:, :, :].rearrange("p a b -> p (a b)")).then_inc(b_chain, 1)
                    chain["n"] += 1
                if kind == "norm" and s[2] == 3:
                    qb = s[1]
                    before = cnt.before
                    dve.wait_ge(ctx_ready, before["norm"] * 2 + (2 * qb + 1))
                    nc.vector.tensor_tensor(cval[:, :], p_val[:, :], rden[:, :], ALU.mult).then_inc(norm_done, 1)

            cnt = Count()
            for s in first:
                run(s, cnt, None, 0, False)
            first_links = chain["n"]
            LINKS = 3 * (NQB) + 4 * NQB

            def body(g, u, before, last):
                base = (g * NU + u) * LINKS + first_links
                chain["base"], chain["n"] = base if last or isinstance(g, int) else dve.snap(base), 0
                cnt = Count(before)
                for s in schedule(last):
                    run(s, cnt, g, u, last)
                assert last or chain["n"] == LINKS

            over_groups(dve, ["bank", "shift", "values", "sum", "norm"], body)

        @block.tensor
        def _(pe):
            pe.sem_inc(values_done, V_CREDIT)
            pe.sem_inc(sums_done, S_CREDIT)
            pe.wait_ge(init_done, NU + 1)

            def run(s, cnt, g, u):
                kind = s[0]
                before = cnt.before
                if kind in ("max", "rows"):
                    own = 0 if g is None else owner(s, u)
                    m, k = cnt.next_bank()
                    k = k if g is None else u * N["bank"] + k
                    out = p_max[mx_ring.slot(k)]
                if kind == "max":
                    _, _, qb, h, t, cb = s
                    diagonal = cb == qb
                    width = P * (t + 1) if diagonal else TB
                    pe.wait_ge(max_taken, m + (1 + S1_BANKS - mx_ring.back(k)))
                    q0 = qb * TB + t * P
                    ins = nc.tensor.matmul(out[:, 0:width], qs[own][0:3 * DH, h, q0:q0 + P],
                                           ks[own][0:3 * DH, cb * TB:cb * TB + width], start=True, stop=not diagonal)
                    if diagonal:
                        ins = nc.tensor.matmul(out[:, width - P:width], c["identb"][:, :], c["mask_qk"][:, :],
                                               start=False, stop=True)
                    ins.then_inc(max_scored, 1)
                if kind == "shift":
                    cnt.shift += 1
                if kind == "rows":
                    _, _, qb, r = s
                    pe.wait_ge(shift_ready, cnt.shifts())
                    pe.wait_ge(max_taken, m + (1 + S1_BANKS - mx_ring.back(k)))
                    for j in range(G * TT // 2):
                        ins = nc.tensor.transpose(rows_view(mx_ring.slot(k))[:, j, :],
                                                  mpair[:, r * (G * TT // 2) + j, :], c["ident16"][:, :])
                    ins.then_inc(max_scored, 1)
                if kind in ("score", "next"):
                    _, qb, kt, h = s
                    n = items["score"].index(("score", qb, kt, h))
                    before = before or {"score": 0, "bank": 0}
                    ahead = N if kind == "next" and g is not None else {"score": 0, "bank": 0}
                    k = (u * N["score"] + n + ahead["score"]) % (NU * N["score"])
                    of = u if g is None or kind == "score" else 1 - u
                    off = P * max(kt - TT * qb, 0)
                    out = p_sc[sc_ring.slot(k)]
                    pe.wait_ge(exp_done, before["score"] + (ahead["score"] + n + 1 + S2_BANKS - sc_ring.back(k)))
                    if kt == 0:
                        pe.wait_ge(max_taken, before["bank"] + (ahead["bank"] + rows_at(qb, h // 2) + S1_BANKS))
                    ins = nc.tensor.matmul(out[:, off:TB], ks[of][:, kt * P:(kt + 1) * P],
                                           qs[of][:, h, qb * TB + off:(qb + 1) * TB], start=True, stop=True)
                    ins.then_inc(scored, 1)
                if kind == "values":
                    _, qb, kt = s
                    off = P * max(kt - TT * qb, 0)
                    step = step_of(qb, kt)
                    if kt == 0:
                        pe.wait_ge(norm_done, before["norm"] + (qb + 1))
                    pe.wait_ge(exp_done, before["score"] + (G * (step + 1) + S2_BANKS))
                    if kt >= TT * qb:
                        pe.wait_ge(masked, before["norm"] * TT + (qb * TT + kt - TT * qb + 1))
                    for h in range(G):
                        ins = nc.tensor.matmul(p_val[h * DH:(h + 1) * DH, off:TB], vs[u][:, kt, :],
                                               prob[:, step % P_GEN, h, off:TB], start=(kt == 0),
                                               stop=(kt == TT * (qb + 1) - 1))
                    ins.then_inc(values_done, 1)
                if kind == "sum":
                    _, qb, kt, size = s
                    off = P * max(kt - TT * qb, 0)
                    step = step_of(qb, kt)
                    mine = [x for x in items["sum"] if x[1] == qb]
                    if size:
                        k = bundles.index(s)
                        done = items["add"].index(("add", k, kt + size - 1)) + 1
                        pe.wait_ge(tile_added, before["add"] * G + (G * done + A_CREDIT))
                    for h in range(G):
                        src = psum[:, k % SUMS, h, :] if size else prob[:, step % P_GEN, h, off:TB]
                        ins = nc.tensor.matmul(p_sum[h * DH:(h + 1) * DH, off:TB], c["ones"][:, :], src,
                                               start=(s == mine[0]), stop=(s == mine[-1]))
                    ins.then_inc(sums_done, 1)

            pe.wait_ge(group_in[0], 7 * 16)
            cnt = Count()
            for s in first + [("next", 0, 0, h) for h in range(G)]:
                run(s, cnt, None, 0)

            def body(g, u, before, last):
                cnt = Count(before)
                fetched = False
                for s in schedule(last):
                    if s[:3] == ("score", 0, 0):
                        continue
                    if s[0] == "max" and s[1] and not fetched:
                        pe.wait_ge(group_in[1 - u], 7 * 16 * (g + 1 + u))
                        fetched = True
                    run(s, cnt, g, u)

            over_groups(pe, list(N), body)



def phase_c(nc, c, x, g_dram, ctx_dram, out):
    wo = c["w_out"]
    HALVES = E // TB
    with ExitStack() as stack:
        sb = lambda name, shape, dt: stack.enter_context(nc.sbuf_tensor(name, shape, dt))
        sem = lambda name: stack.enter_context(nc.semaphore(name))
        cx = sb("cx", [P, 2, 2, HKV, TB], F16)
        xin = sb("x_again", [P, TT, E], F32)
        gin = sb("gin", [P, TT, E], F32)
        res = sb("res", [P, TT, E], F32)
        acc = [stack.enter_context(nc.psum_tensor(f"out_acc{i}", [P, TB], F32)) for i in range(ACC)]
        cx_in = [sem(f"cx_in{u}") for u in range(2)]
        xg_in = [sem(f"xg_in{t}") for t in range(TT)]
        stored = [sem(f"out_stored{t}") for t in range(TT)]
        group_done, gated, res_done = sem("c_group_done"), sem("gated"), sem("res_done")
        passed = sem("passed_c")
        block = stack.enter_context(nc.Block())
        PER = TT * HALVES

        def over_blocks(eng, body):
            with eng.Fori(0, NBLK // 2) as i:
                body(2 * i, i, 0)
                body(2 * i + 1, i, 1)

        @block.sync
        def _(sp):
            def body(nb, i, u):
                sp.wait_ge(group_done, nb * PER + 1)
                sp.sem_inc(passed, 1)
                for part in range(2):
                    sp.dma_start(cx[:, u, part, :, :],
                                 ctx_dram[:, :, part, bass.ds(nb * TB, TB)].rearrange("g p t -> p g t")
                                 ).then_inc(cx_in[u], 16)
                for t in range(TT):
                    sp.wait_ge(res_done, nb * TT + t + 1)
                    sp.sem_inc(passed, 1)
                    rows = bass.ds(nb * TB + t * P, P)
                    sp.dma_start(xin[:, t, :], x[rows, :]).then_inc(xg_in[t], 16)
                    sp.dma_start(gin[:, t, :], g_dram[rows, :]).then_inc(xg_in[t], 16)

            over_blocks(sp, body)

        @block.tensor
        def _(pe):
            pe.sem_inc(group_done, PER + 1)

            def body(nb, i, u):
                pe.wait_ge(cx_in[u], 32 * (i + 1))
                for t in range(TT):
                    for half in range(HALVES):
                        n = t * HALVES + half
                        bank = acc[n % ACC]
                        pe.wait_ge(gated, nb * PER + n + 1)
                        order = [(a, b, g) for g in range(HKV) for a, b in ((0, 0), (0, 1), (1, 0))]
                        for m, (a, b, g) in enumerate(order):
                            ins = nc.tensor.matmul(bank[:, :], cx[:, u, a, g, t * P:(t + 1) * P],
                                                   wo[:, b, g, half * TB:(half + 1) * TB],
                                                   start=(m == 0), stop=(m == len(order) - 1))
                        ins.then_inc(group_done, 1)

            over_blocks(pe, body)

        @block.vector
        def _(dve):
            dve.sem_inc(gated, ACC)
            dve.sem_inc(res_done, TT)

            def body(nb, i, u):
                for t in range(TT):
                    dve.wait_ge(xg_in[t], 32 * (nb + 1))
                    dve.wait_ge(stored[t], 16 * nb + 16)
                    for half in range(HALVES):
                        n = t * HALVES + half
                        cols = slice(half * TB, (half + 1) * TB)
                        dve.wait_ge(group_done, nb * PER + n + 2 + PER)
                        nc.vector.scalar_tensor_tensor(out=res[:, t, cols], in0=acc[n % ACC][:, :],
                                                       scalar=c["out_scale"][:, 0:1], in1=gin[:, t, cols],
                                                       op0=ALU.mult, op1=ALU.mult).then_inc(gated, 1)
                    dve.wait_ge(gated, nb * PER + (t + 1) * HALVES + ACC)
                    nc.vector.tensor_tensor(res[:, t, :], res[:, t, :], xin[:, t, :], ALU.add).then_inc(res_done, 1)

            over_blocks(dve, body)

        @block.scalar
        def _(act):
            for t in range(TT):
                act.sem_inc(stored[t], 16)

            def body(nb, i, u):
                for t in range(TT):
                    act.wait_ge(res_done, nb * TT + t + 1 + TT)
                    act.dma_start(out[bass.ds(nb * TB + t * P, P), :], res[:, t, :]).then_inc(stored[t], 16)

            over_blocks(act, body)
            for t in range(TT):
                act.wait_ge(stored[t], 16 * NBLK + 16)



def program(nc, x, wq, wk, wv, wo, qw, sw, bias, tables, out):
    q_dram = nc.dram_tensor("q_pairs", [QT, P, 2, NTOK], F16, kind="Internal").ap()
    k_dram = nc.dram_tensor("k_pairs", [HKV, DH, 2, NTOK], F16, kind="Internal").ap()
    v_dram = nc.dram_tensor("v_tiles", [HKV, P, NTOK // P, DH], F32, kind="Internal").ap()
    g_dram = nc.dram_tensor("gate", [NTOK, E], F32, kind="Internal").ap()
    ctx_dram = nc.dram_tensor("context_pairs", [HKV, P, 2, NTOK], F16, kind="Internal").ap()
    wo_pairs = nc.dram_tensor("wo_pairs", [P, 2, KC, E], F16, kind="Internal").ap()
    with ExitStack() as stack:
        sb = lambda name, shape, dt: stack.enter_context(nc.sbuf_tensor(name, shape, dt))
        sem = lambda name: stack.enter_context(nc.semaphore(name))
        c = {"sem": sem}
        c["ident16"] = sb("ident16", [P, P], F16)
        c["identb"] = sb("identb", [P, P], BF16)
        c["mask_qk"] = sb("mask_qk", [P, P], BF16)
        c["ones"] = sb("ones", [P, DH], F32)
        build_constants(nc, c)
        unit, inv = sb("unit", [P, 5], F32), sb("inv", [P, 5], F32)
        swt = sb("swt", [P, 1], F32)
        for name in ("gate_scale", "exp_scale", "out_scale"):
            c[name] = sb(name, [P, 1], F32)
        c["gate_rest"] = sb("gate_rest", [P, 1], I32)
        with ExitStack() as early:
            esb = lambda name, shape, dt: early.enter_context(nc.sbuf_tensor(name, shape, dt))
            c["w_qkv"] = esb("w_qkv", [P, 2, KC, NQKV], F16)
            c["w_gate"] = esb("w_gate", [P, 2, KC, E], F16)
            with nc.sbuf_tensor("w_out_early", [P, 2, KC, E], F16) as c["w_out"]:
                prepare_weights(nc, c, [(wq, c["w_qkv"], 0, 0), (wk, c["w_qkv"], E, QT),
                                        (wv, c["w_qkv"], E + HKV * DH, QT + KT),
                                        (wo, c["w_out"], 0, QT + 2 * KT), (qw, c["w_gate"], 0, 0)],
                                unit, inv, wo_pairs)
            c["bias"] = esb("bias", [P, E], F32)
            small_in, scales = sem("small_in"), sem("scales")
            with nc.Block() as block:

                @block.sync
                def _(sp):
                    sp.dma_start(c["bias"][:, :], bias).then_inc(small_in, 16)
                    sp.dma_start(swt[:, :], sw).then_inc(small_in, 16)

                @block.vector
                def _(dve):
                    dve.wait_ge(small_in, 32)
                    nc.vector.memset(c["ones"][:, :], 1.0).then_inc(scales, 1)
                    nc.vector.scalar_tensor_tensor(out=c["gate_scale"][:, :], in0=inv[:, 4:5], scalar=1.0 / X_UP,
                                                   in1=swt[:, :], op0=ALU.mult, op1=ALU.mult).then_inc(scales, 1)
                    nc.vector.scalar_tensor_tensor(out=c["exp_scale"][:, :], in0=inv[:, 0:1],
                                                   scalar=float(DH ** -0.5 / (X_UP * Q_DOWN) ** 2), in1=inv[:, 1:2],
                                                   op0=ALU.mult, op1=ALU.mult).then_inc(scales, 1)
                    nc.vector.scalar_tensor_tensor(out=c["out_scale"][:, :], in0=inv[:, 2:3],
                                                   scalar=1.0 / (X_UP * V_DOWN), in1=inv[:, 3:4],
                                                   op0=ALU.mult, op1=ALU.mult).then_inc(scales, 1)
                    dve.wait_ge(scales, 4)

            phase_a(nc, c, x, tables, q_dram, k_dram.rearrange("(a g) d s t -> a (g d) s t", a=KT), v_dram, g_dram)
        c["w_out"] = sb("w_out", [P, 2, KC, E], F16)
        nc.disable_value_cache = True
        phase_b(nc, c, q_dram, k_dram, v_dram, ctx_dram, wo_pairs)
        nc.disable_value_cache = False
        phase_c(nc, c, x, g_dram, ctx_dram, out)


def kernel(**inputs):
    import concourse.bacc as bacc
    from concourse.bass_utils import run_bass_kernel_spmd

    nc = bacc.Bacc("TRN2", target_bir_lowering=False, num_devices=1)
    arrays, args = {}, []

    def add(name, a):
        a = np.ascontiguousarray(a)
        arrays[f"in_{name}"] = a
        args.append(nc.dram_tensor(f"in_{name}", a.shape, mybir.dt.from_np(a.dtype), kind="ExternalInput").ap())

    x = np.asarray(inputs["L0_attn_x"])
    add("x", x.reshape(NTOK, E))
    for name in ("L0_attn_Wq", "L0_attn_Wk", "L0_attn_Wv", "L0_attn_Wo", "L0_ffn_qw"):
        add(name, np.asarray(inputs[name]))
    add("sw", np.broadcast_to(np.asarray(inputs["L0_ffn_sw"]).reshape(1, 1), (P, 1)))
    add("bias", np.broadcast_to(np.asarray(inputs["L0_ffn_bias"]).reshape(1, E), (P, E)))
    add("tables", rope_tables())
    args.append(nc.dram_tensor("out", [NTOK, E], F32, kind="ExternalOutput").ap())
    program(nc, *args)
    r = run_bass_kernel_spmd(nc, [arrays], core_ids=[0])
    return r.results[0]["out"].reshape(x.shape)
```
